# Optimizing a Trainium2 kernel written in Bass

```python
import numpy as np
import jax
import jax.numpy as jnp

def _softmax(x, axis=-1):
    return jax.nn.softmax(x, axis=axis)

def _gelu(x):
    return jax.nn.gelu(x, approximate=True)

def _silu(x):
    return jax.nn.silu(x)

def _sigmoid(x):
    return jax.nn.sigmoid(x)

def _layernorm(x, axis=-1, eps=1e-05):
    m = jnp.mean(x, axis=axis, keepdims=True)
    v = jnp.var(x, axis=axis, keepdims=True)
    return (x - m) / jnp.sqrt(v + eps)

def _scatter_add(tgt, idx, src, axis=0):
    return tgt.at[idx].add(src)

def _segment_sum(src, seg, n):
    return jax.ops.segment_sum(src, seg, n)
kernel_name = 'mk_sandwich_d1_jaxref_r8_d6efd1'

def setup_inputs(seed: int=0):
    np.random.seed(seed)
    _w = jnp.asarray

    def _L0_attn_setup():
        import jax, jax.numpy as jnp
        import numpy as np
        K_FACTOR = 0.5
        key = jax.random.key(seed)
        k1, k2, k3, k4 = jax.random.split(key, 4)
        B, S, H, I = (1, 256, 512, 1376)
        x = jax.random.normal(k1, (B, S, H), dtype=jnp.float32)
        w_gate = jax.random.normal(k2, (I, H), dtype=jnp.float32) * 0.02
        w_up = jax.random.normal(k3, (I, H), dtype=jnp.float32) * 0.02
        w_down = jax.random.normal(k4, (H, I), dtype=jnp.float32) * 0.02
        return {'x': x, 'w_gate': w_gate, 'w_up': w_up, 'w_down': w_down}
    _L0_attn_in = _L0_attn_setup()

    def _L0_ffn_setup():
        import jax, jax.numpy as jnp
        import numpy as np
        D = 512
        F = 1376
        B, S = (4, 256)
        key = jax.random.key(seed)
        k_x, k_g, k_u, k_d = jax.random.split(key, 4)
        scale = 0.02
        return {'x': jax.random.normal(k_x, (B, S, D), dtype=jnp.float32), 'W_gate': jax.random.normal(k_g, (F, D), dtype=jnp.float32) * scale, 'W_up': jax.random.normal(k_u, (F, D), dtype=jnp.float32) * scale, 'W_down': jax.random.normal(k_d, (D, F), dtype=jnp.float32) * scale}
    _L0_ffn_in = _L0_ffn_setup()
    _d = {'L0_attn_x': _L0_attn_in['x'], 'L0_attn_w_gate': _L0_attn_in['w_gate'], 'L0_attn_w_up': _L0_attn_in['w_up'], 'L0_attn_w_down': _L0_attn_in['w_down'], 'L0_ffn_W_gate': _L0_ffn_in['W_gate'], 'L0_ffn_W_up': _L0_ffn_in['W_up'], 'L0_ffn_W_down': _L0_ffn_in['W_down']}
    _x0 = _d['L0_attn_x']
    _d['L0_attn_x'] = jax.random.normal(jax.random.fold_in(jax.random.key(seed), 1), (4, 512, 512), dtype=_x0.dtype)
    del _x0
    return _d

def reference(L0_attn_x, L0_attn_w_gate, L0_attn_w_up, L0_attn_w_down, L0_ffn_W_gate, L0_ffn_W_up, L0_ffn_W_down):

    def _L0_attn_ref(x, w_gate, w_up, w_down):
        import jax, jax.numpy as jnp
        import numpy as np
        K_FACTOR = 0.5
        s = jax.nn.silu(jnp.einsum('bsh,ih->bsi', x, w_gate))
        B, S, I = s.shape
        k = int(K_FACTOR * I)
        _, idx = jax.lax.top_k(-jnp.abs(s), k)
        flat = s.reshape(B * S, I)
        rows = jnp.arange(B * S)[:, None]
        flat = flat.at[rows, idx.reshape(B * S, k)].set(0.0)
        s = flat.reshape(B, S, I)
        s = s * jnp.einsum('bsh,ih->bsi', x, w_up)
        return jnp.einsum('bsi,hi->bsh', s, w_down)

    def _L0_ffn_ref(x, W_gate, W_up, W_down):
        import jax, jax.numpy as jnp
        import numpy as np
        D = 512
        F = 1376
        B, S = (4, 256)
        out_shape = x.shape[:-1] + (W_down.shape[0],)
        xt = x.reshape(-1, x.shape[-1])
        up = xt @ W_up.T
        gate = jax.nn.silu(xt @ W_gate.T)
        y = gate * up @ W_down.T
        return y.reshape(out_shape)
    x = L0_attn_x
    x = x + _layernorm(_L0_attn_ref(_layernorm(x, axis=-1), L0_attn_w_gate, L0_attn_w_up, L0_attn_w_down), axis=-1)
    x = x + _layernorm(_L0_ffn_ref(_layernorm(x, axis=-1), L0_ffn_W_gate, L0_ffn_W_up, L0_ffn_W_down), axis=-1)
    return x

_drawn_inputs = setup_inputs


def setup_inputs(seed=0):
    import zlib

    import numpy as np

    out = dict(_drawn_inputs(seed))
    spreads = {}
    factors = {}
    for name, (base, spread) in spreads.items():
        noise = np.random.default_rng([zlib.crc32(name.encode()), seed]).standard_normal(out[name].shape)
        drawn = base * np.exp(spread * noise) if base else spread * noise
        out[name] = jnp.asarray(drawn.astype(out[name].dtype))
    for name, factor in factors.items():
        out[name] = (out[name] * factor).astype(out[name].dtype)
    return out
```

```python
import numpy as np
import concourse.bass as bass
from concourse import mybir
from contextlib import ExitStack

F32 = mybir.dt.float32
F32R = mybir.dt.float32r
BF16 = mybir.dt.bfloat16
I32 = mybir.dt.int32
ALU = mybir.AluOpType
ACT = mybir.ActivationFunctionType
AX = mybir.AxisListType

P = 128


class Tile:

    def __init__(self, i, m, c):
        self.i, self.m, self.c = i, m, c

    def __add__(self, n):
        return Tile(self.i, self.m + n.m, self.c + n.c) if isinstance(n, Tile) else Tile(self.i, self.m, self.c + n)

    def __sub__(self, n):
        return Tile(self.i, self.m, self.c - n)

    def __mul__(self, n):
        return Tile(self.i, self.m * n, self.c * n)

    __radd__, __rmul__ = __add__, __mul__


def at(n):
    return n.i * n.m + n.c if isinstance(n, Tile) else n


def sandwich(nc, x, w_gate, w_up, w_down, W_gate, W_up, W_down, out):
    B, S, H = x.shape
    I = w_gate.shape[0]
    TOK = B * S
    TILES = TOK // P
    KC = H // P
    JC = -(-I // P)
    LASTJ = I - (JC - 1) * P
    IP = JC * P
    CW = [460, 460, 456]
    CO = [0, 460, 920]
    TG = [(0, 4), (4, 4), (8, 3)]
    assert sum(CW) == I and H == 512 and TOK % (2 * P) == 0 and I == 1376
    EPS = 1e-5

    K = I // 2
    WINDOW = 8
    AIM = K + (WINDOW - 1) / 2
    GUESS, DENSITY = 0.79, 0.63
    GAIN = [1.0, 1.0, 0.7, 0.5, 0.7]
    STEPS = len(GAIN)

    xf = x.rearrange("b s h -> (b s) h")
    of = out.rearrange("b s h -> (b s) h")
    x1 = nc.dram_tensor("x1_scratch", (TOK, H), F32, kind="Internal").ap()
    weights = [(w_gate, w_up, w_down), (W_gate, W_up, W_down)]

    ctx = ExitStack()
    with ctx:
        def sb(name, shape, dt=F32):
            return ctx.enter_context(nc.sbuf_tensor(name, shape, dt))

        def sem(name):
            return ctx.enter_context(nc.semaphore(name))

        gu_hi = [sb(n, [P, KC, I], F32R) for n in ("gate_hi", "up_hi")]
        gu_lo = [sb(n, [P, KC, I], F32R) for n in ("gate_lo", "up_lo")]
        down_hi = sb("down_hi", [P, JC, H], F32R)
        down_lo = sb("down_lo", [P, JC, H], F32R)
        NSTAGE = 7
        stage = sb("stage", [P, NSTAGE, H])
        ident = sb("ident", [P, P])
        xin = sb("xin", [P, 2, H])
        xres = sb("xres", [P, 2, H])
        xT_hi = [sb(f"xT_hi{i}", [P, KC, P], F32R) for i in range(2)]
        xT_lo = [sb(f"xT_lo{i}", [P, KC, P], F32R) for i in range(2)]
        absv = sb("absv", [P, 2, I])
        prod = sb("prod", [P, 2, IP])
        below = sb("below", [P, I])
        junk = sb("junk", [P, I], BF16)
        hT_hi = sb("hT_hi", [P, JC, P], F32R)
        hT_lo = sb("hT_lo", [P, JC, P], F32R)

        xstat = sb("xstat", [P, 6])
        xmv = sb("xmv", [P, 2])
        xrstd = sb("xrstd", [P, 2])
        ystat = sb("ystat", [P, 6])
        ymv = sb("ymv", [P, 2])
        yrstd = sb("yrstd", [P, 2])
        ybias = sb("ybias", [P, 1])
        half = sb("half", [P, 1])
        asum = sb("asum", [P, 2])
        gains = sb("gains", [P, STEPS])
        unit = sb("unit", [P, STEPS])
        thr = sb("thr", [P, 2])
        sgn = sb("sgn", [P, 2])
        err = sb("err", [P, 1])
        ymean = sb("ymean", [P, 1])
        move = sb("move", [P, 1])
        delta = sb("delta", [P, 1])
        rank = sb("rank", [P, 1])
        tied = sb("tied", [P, 1])
        top = sb("top", [P, 8])
        iota = sb("iota", [P, 2, 8])
        pick = sb("pick", [P, 2, 8])
        kth = sb("kth", [P, 1])
        nxt = sb("nxt", [P, 1])
        flag = sb("flag", [P, 32])
        flagT = sb("flagT", [P, 32])
        flagq = sb("flagq", [P, 4])
        anyflag = sb("anyflag", [P, 1], I32)
        ebit = sb("ebit", [P, 1])
        ecnt = sb("ecnt", [P, 1])
        eadd = sb("eadd", [P, 1], I32)
        ecand = sb("ecand", [P, 1], I32)
        eth = sb("eth", [P, 1], I32)

        gu_ps = [ctx.enter_context(nc.psum_tensor(f"gu_ps{i}", [P, 512], F32)) for i in range(4)]
        tr_ps = [ctx.enter_context(nc.psum_tensor(f"tr_ps{i}", [P, 4, P], F32)) for i in range(3)]
        y_ps = ctx.enter_context(nc.psum_tensor("y_ps", [P, H], F32))

        stage_in = [sem(f"stage_in{i}") for i in range(NSTAGE)]
        w_tr, whi_done, wlo_done = sem("w_tr"), sem("whi_done"), sem("wlo_done")
        x_in = [sem(f"x_in{i}") for i in range(2)]
        xres_in = [sem(f"xres_in{i}") for i in range(2)]
        stored = [sem(f"stored{i}") for i in range(2)]
        consts = sem("consts")
        g_done, u_done, x_tr, h_tr, y_done = map(sem, ("g_done", "u_done", "x_tr", "h_tr", "y_done"))
        silu_done, xhi_done, hhi_done, ynorm_done, counted = map(
            sem, ("silu_done", "xhi_done", "hhi_done", "ynorm_done", "counted"))
        a_done, p_done, xn_done, xlo_done, hlo_done, res_done = map(
            sem, ("a_done", "p_done", "xn_done", "xlo_done", "hlo_done", "res_done"))
        xst, xag, yst, yag = map(sem, ("xst", "xag", "yst", "yag"))
        below_done, top_done, rank_done, pick_done, flag_done, flagT_done, any_done, h_done = map(
            sem, ("below_done", "top_done", "rank_done", "pick_done", "flag_done", "flagT_done",
                  "any_done", "h_done"))
        xr_done, yr_done, thr_done, pool_step = map(sem, ("xr_done", "yr_done", "thr_done", "pool_step"))
        exact = sem("exact")
        passed = sem("passed")

        block = ctx.enter_context(nc.Block())

        T2 = 2 * TILES

        def pipeline(eng, step, weights_gu=None, weights_down=None):
            nothing = lambda b: None
            wgu, wdn = weights_gu or nothing, weights_down or nothing
            for b in range(2):
                j0 = b * TILES
                wgu(b)
                if b == 0:
                    wdn(b)
                step(j0, 0, b, prev=b - 1 if b else None, next_=b)
                if b == 1:
                    wdn(b)
                if b == 0:
                    step(1, 1, b, prev=b, next_=b)
                    step(2, 0, b, prev=b, next_=b)
                first = j0 + (3 if b == 0 else 1)
                with eng.Fori(0, (j0 + TILES - 1 - first) // 2) as i:
                    j = Tile(i, 2, first)
                    step(j, 1, b, prev=b, next_=b)
                    step(j + 1, 0, b, prev=b, next_=b)
                step(j0 + TILES - 1, 1, b, prev=b, next_=b + 1 if b == 0 else None)
            step(T2, 0, None, prev=1, next_=None)

        def wnum(b, n):
            return b * 3 * JC + n

        @block.sync
        def _(sp):
            def rows(t, j, b):
                return t[bass.ds(at((j - b * TILES) * P), P), :]

            def load_x(j, par, b):
                if not isinstance(j, int) or j >= 2:
                    sp.wait_ge(x_tr, at(j - 1))
                if b == 1:
                    sp.wait_ge(stored[par], at((j - TILES - par) * 8 + 16))
                sp.dma_start(xin[:, par, :], rows(xf if b == 0 else x1, j, b)).then_inc(x_in[par], 16)

            def load_w(b, n):
                w, s = wnum(b, n), wnum(b, n) % NSTAGE
                if w >= NSTAGE:
                    sp.wait_ge(w_tr, w - NSTAGE + 1)
                m, c = divmod(n, JC)
                size = P if c < JC - 1 else LASTJ
                if m < 2:
                    src, dst = weights[b][m][c * P:c * P + size, :], stage[0:size, s, :]
                else:
                    src = weights[b][2][:, c * P:c * P + size].rearrange("(r p) q -> p r q", p=P)
                    dst = stage[:, s, :].rearrange("p (r q) -> p r q", q=P)[:, :, 0:size]
                sp.dma_start(dst, src).then_inc(stage_in[s], 16)

            def store(j, par, b):
                sp.wait_ge(res_done, at(j + 1))
                sp.dma_start(rows(x1 if b == 0 else of, j, b), xres[:, par, :]).then_inc(stored[par], 16)

            def load_res(j, par, b):
                if not isinstance(j, int) or j >= 2:
                    sp.wait_ge(stored[par], at((j - par) * 8))
                sp.dma_start(xres[:, par, :], rows(xf if b == 0 else x1, j, b)).then_inc(xres_in[par], 16)

            def step(j, par, b, prev, next_):
                if next_ is not None and not (isinstance(j, int) and j == 0):
                    load_x(j + 1, 1 - par, next_)
                if not isinstance(j, int):
                    store(j - 2, par, b)
                elif j >= 2:
                    store(j - 2, par, (j - 2) // TILES)
                if prev is not None:
                    load_res(j - 1, 1 - par, prev)

            load_x(0, 0, 0)
            load_x(1, 1, 0)
            for b in range(2):
                j0 = b * TILES
                for n in range(3 * JC if b == 0 else 2 * JC):
                    load_w(b, n)
                step(j0, 0, b, b - 1 if b else None, b)
                if b == 1:
                    for n in range(2 * JC, 3 * JC):
                        load_w(b, n)
                step(j0 + 1, 1, b, b, b)
                step(j0 + 2, 0, b, b, b)
                with sp.Fori(0, TILES // 2 - 2) as i:
                    j = Tile(i, 2, j0 + 3)
                    step(j, 1, b, b, b)
                    step(j + 1, 0, b, b, b)
                step(j0 + TILES - 1, 1, b, b, b + 1 if b == 0 else None)
            step(T2, 0, 1, 1, None)
            store(T2 - 1, 1, 1)
            for i in range(2):
                sp.wait_ge(stored[i], 16 * TILES)

        @block.tensor
        def _(pe):
            def transpose_weights(b, first, count):
                for n in range(first, first + count):
                    w = wnum(b, n)
                    m, c = divmod(n, JC)
                    size = P if c < JC - 1 else LASTJ
                    pe.wait_ge(stage_in[w % NSTAGE], 16 * (w // NSTAGE + 1))
                    if n - first < 3:
                        if w >= 3:
                            pe.wait_ge(wlo_done, w - 2 if n - first else w)
                        if b == 1 or first:
                            t = b * TILES
                            if b == 1 and first == 0:
                                pe.wait_ge(hlo_done, 3 * (t - 1))
                                pe.wait_ge(xlo_done, t + 1)
                            elif b == 1:
                                pe.wait_ge(hlo_done, 3 * t)
                                pe.wait_ge(xlo_done, t + 2)
                        elif n == 0:
                            pe.wait_ge(xlo_done, 1)
                    else:
                        pe.wait_ge(wlo_done, w - 2)
                    s = w % NSTAGE
                    for r in range(KC):
                        if m < 2:
                            last = nc.tensor.transpose(tr_ps[w % 3][:, r, 0:size],
                                                       stage[0:size, s, r * P:(r + 1) * P],
                                                       ident[0:size, 0:size])
                        else:
                            last = nc.tensor.transpose(tr_ps[w % 3][0:size, r, :],
                                                       stage[:, s, r * P:r * P + size], ident[:, :])
                    last.then_inc(w_tr, 1)

            def transpose_x(j, par, wait_h):
                pe.wait_ge(xn_done, at(j + 1))
                if wait_h is not None:
                    pe.wait_ge(hlo_done, at(wait_h))
                for c in range(KC):
                    last = nc.tensor.transpose(tr_ps[0][:, c, :], xin[:, par, c * P:(c + 1) * P], ident[:, :])
                last.then_inc(x_tr, 1)

            def product(j, par, m, n):
                q = (3 * m + n) + 2 * par
                bank = gu_ps[q % 4]
                first = isinstance(j, int) and j == 0
                if (m, n) == (0, 0) and not first:
                    pe.wait_ge(silu_done, at(3 * j))
                elif m == 0 and not first:
                    pe.wait_ge(p_done, at(3 * j - 3 + n))
                elif (m, n) == (1, 0) and not first:
                    pe.wait_ge(p_done, at(3 * j))
                elif m == 1 and n > 0:
                    pe.wait_ge(silu_done, at(3 * j + n))
                cols = slice(CO[n], CO[n] + CW[n])
                for c in range(KC):
                    for i, (xt, w) in enumerate(((xT_hi, gu_lo), (xT_lo, gu_hi), (xT_hi, gu_hi))):
                        last = nc.tensor.matmul(bank[:, 0:CW[n]], xt[par][:, c, :], w[m][:, c, cols],
                                                start=(c == 0 and i == 0), stop=(c == KC - 1 and i == 2))
                last.then_inc((g_done, u_done)[m], 1)

            def transpose_h(j, par, blk):
                if blk == 0:
                    pe.wait_ge(h_done, at(j + 1))
                else:
                    pe.wait_ge(p_done, at(3 * j + 3))
                for g, (c0, cn) in enumerate(TG):
                    for c in range(cn):
                        last = nc.tensor.transpose(tr_ps[g][:, c, :],
                                                   prod[:, par, (c0 + c) * P:(c0 + c + 1) * P], ident[:, :])
                    last.then_inc(h_tr, 1)

            def down(j):
                if not isinstance(j, int) or j >= 1:
                    pe.wait_ge(res_done, at(j))
                for g, (c0, cn) in enumerate(TG):
                    pe.wait_ge(hlo_done, at(3 * j + g + 1))
                    for c in range(c0, c0 + cn):
                        k = P if c < JC - 1 else LASTJ
                        for i, (h, w) in enumerate(((hT_hi, down_lo), (hT_lo, down_hi), (hT_hi, down_hi))):
                            last = nc.tensor.matmul(y_ps[:, :], h[0:k, c, :], w[0:k, c, :],
                                                    start=(c == 0 and i == 0),
                                                    stop=(c == JC - 1 and i == 2))
                last.then_inc(y_done, 1)

            def step(j, par, b, prev, next_):
                static = isinstance(j, int)
                if b is not None:
                    if static and j % TILES == 0:
                        pe.wait_ge(xlo_done, at(j + 1))
                        product(j, par, 0, 0)
                    product(j, par, 0, 1)
                    product(j, par, 0, 2)
                    if next_ is not None:
                        transpose_x(j + 1, 1 - par, None if static and j < 2 else 3 * (j - 1))
                    for n in range(3):
                        product(j, par, 1, n)
                if prev is not None:
                    if next_ is not None:
                        pe.wait_ge(xlo_done, at(j + 2))
                    if not static or j >= 2:
                        pe.wait_ge(hlo_done, at(3 * (j - 1)))
                    transpose_h(j - 1, 1 - par, prev)
                if next_ is not None and next_ == b:
                    pe.wait_ge(xlo_done, at(j + 2))
                    product(j + 1, 1 - par, 0, 0)
                if prev is not None:
                    down(j - 1)

            pe.wait_ge(consts, CONSTS)
            transpose_x(0, 0, None)

            def wgu(b):
                transpose_weights(b, 0, 2 * JC)
                pe.wait_ge(wlo_done, wnum(b, 2 * JC))

            def wdn(b):
                transpose_weights(b, 2 * JC, JC)
                pe.wait_ge(wlo_done, wnum(b, 3 * JC))

            pipeline(pe, step, wgu, wdn)

        @block.scalar
        def _(act):
            def split_weights_hi(b, first, count):
                for n in range(first, first + count):
                    w = wnum(b, n)
                    m, c = divmod(n, JC)
                    size = P if c < JC - 1 else LASTJ
                    if b == 1 and n == first:
                        if m == 0:
                            act.wait_ge(g_done, 3 * TILES)
                            act.wait_ge(u_done, 3 * TILES)
                        else:
                            act.wait_ge(y_done, TILES)
                    act.wait_ge(w_tr, w + 1)
                    if m < 2:
                        src, dst = tr_ps[w % 3][:, :, 0:size], gu_hi[m][:, :, c * P:c * P + size]
                    else:
                        src = tr_ps[w % 3][0:size, :, :].rearrange("q r p -> q (r p)")
                        dst = down_hi[0:size, c, :]
                    nc.scalar.activation(dst, src, ACT.Copy).then_inc(whi_done, 1)

            def count(j, par, n):
                act.wait_ge(thr_done, at(STEPS * j + j + n + 1))
                nc.scalar.activation(junk[:, :], absv[:, par, :], ACT.Sign, bias=thr[:, par:par + 1],
                                     scale=-1.0, accum_out=sgn[:, par:par + 1]).then_inc(counted, 1)

            def silu(j, par, n):
                act.wait_ge(g_done, at(3 * j + n + 1))
                if n == 0 and (not isinstance(j, int) or j >= 2):
                    act.wait_ge(h_tr, at(3 * (j - 1)))
                q = n + 2 * par
                nc.scalar.activation(prod[:, par, CO[n]:CO[n] + CW[n]], gu_ps[q % 4][:, 0:CW[n]],
                                     ACT.Silu).then_inc(silu_done, 1)

            def split_x_hi(j, par):
                act.wait_ge(x_tr, at(j + 1))
                if not isinstance(j, int) or j >= 2:
                    act.wait_ge(u_done, at(3 * (j - 1)))
                nc.scalar.activation(xT_hi[par][:, :, :], tr_ps[0][:, :, :], ACT.Copy).then_inc(xhi_done, 1)

            def split_h_hi(j):
                for g, (c0, cn) in enumerate(TG):
                    act.wait_ge(h_tr, at(3 * j + g + 1))
                    if g == 0 and (not isinstance(j, int) or j >= 1):
                        act.wait_ge(y_done, at(j))
                    nc.scalar.activation(hT_hi[:, c0:c0 + cn, :], tr_ps[g][:, 0:cn, :],
                                         ACT.Copy).then_inc(hhi_done, 1)

            def normalise_y(j):
                act.wait_ge(yr_done, at(j + 1))
                nc.scalar.activation(y_ps[:, :], y_ps[:, :], ACT.Identity, bias=ybias[:, 0:1],
                                     scale=yrstd[:, 0:1]).then_inc(ynorm_done, 1)

            def step(j, par, b, prev, next_):
                static = isinstance(j, int)
                if b is not None:
                    if static and j % TILES == 0:
                        silu(j, par, 0)
                    silu(j, par, 1)
                    silu(j, par, 2)
                if next_ is not None:
                    split_x_hi(j + 1, 1 - par)
                if not static or j >= 2:
                    normalise_y(j - 2)
                if b == 0:
                    for n in range(3):
                        count(j, par, n)
                if prev is not None:
                    split_h_hi(j - 1)
                if next_ is not None and next_ == b:
                    silu(j + 1, 1 - par, 0)
                if b == 0:
                    for n in range(3, STEPS + 1):
                        count(j, par, n)

            split_x_hi(0, 0)
            pipeline(act, step, lambda b: split_weights_hi(b, 0, 2 * JC),
                     lambda b: split_weights_hi(b, 2 * JC, JC))
            normalise_y(T2 - 1)

        @block.vector
        def _(dve):
            for n in range(8):
                nc.vector.memset(iota[:, 0, n:n + 1], float(n))
                nc.vector.memset(iota[:, 1, n:n + 1], float(n + 1) if n < 7 else -1e6)
            for n, g in enumerate(GAIN):
                nc.vector.memset(gains[:, n:n + 1], g)
            nc.vector.memset(flag[:, :], 0.0)
            nc.vector.memset(prod[:, :, I:IP], 0.0)
            nc.vector.memset(half[:, :], -0.5).then_inc(consts, 1)
            dve.wait_ge(consts, CONSTS)

            def split_weights_lo(b, first, count):
                for n in range(first, first + count):
                    w = wnum(b, n)
                    m, c = divmod(n, JC)
                    size = P if c < JC - 1 else LASTJ
                    dve.wait_ge(whi_done, w + 1)
                    if m < 2:
                        src, cols = tr_ps[w % 3][:, :, 0:size], slice(c * P, c * P + size)
                        hi, lo = gu_hi[m][:, :, cols], gu_lo[m][:, :, cols]
                    else:
                        src = tr_ps[w % 3][0:size, :, :].rearrange("q r p -> q (r p)")
                        hi, lo = down_hi[0:size, c, :], down_lo[0:size, c, :]
                    nc.vector.tensor_tensor(lo, src, hi.bitcast(F32), ALU.subtract).then_inc(wlo_done, 1)

            def x_stats(j, par):
                dve.wait_ge(x_in[par], at((j - par) * 8 + 16))
                if not isinstance(j, int) or j >= 1:
                    dve.wait_ge(xn_done, at(j))
                nc.vector.bn_stats(xstat[:, :], xin[:, par, :]).then_inc(xst, 1)
                dve.wait_ge(xst, at(j + 1))
                dve.sem_inc(passed)
                nc.vector.bn_aggr(xmv[:, :], xstat[:, :]).then_inc(xag, 1)

            def x_normalise(j, par):
                dve.wait_ge(xr_done, at(j + 1))
                nc.vector.tensor_scalar(xin[:, par, :], xin[:, par, :], xmv[:, 0:1], xrstd[:, 1:2],
                                        ALU.subtract, ALU.mult).then_inc(xn_done, 1)

            def split_x_lo(j, par):
                dve.wait_ge(xhi_done, at(j + 1))
                nc.vector.tensor_tensor(xT_lo[par][:, :, :], tr_ps[0][:, :, :],
                                        xT_hi[par][:, :, :].bitcast(F32), ALU.subtract).then_inc(xlo_done, 1)

            def split_h_lo(j):
                for g, (c0, cn) in enumerate(TG):
                    dve.wait_ge(hhi_done, at(3 * j + g + 1))
                    nc.vector.tensor_tensor(hT_lo[:, c0:c0 + cn, :], tr_ps[g][:, 0:cn, :],
                                            hT_hi[:, c0:c0 + cn, :].bitcast(F32),
                                            ALU.subtract).then_inc(hlo_done, 1)

            def y_stats(j):
                dve.wait_ge(y_done, at(j + 1))
                nc.vector.bn_stats(ystat[:, :], y_ps[:, :]).then_inc(yst, 1)
                dve.wait_ge(yst, at(j + 1))
                dve.sem_inc(passed)
                nc.vector.bn_aggr(ymv[:, :], ystat[:, :]).then_inc(yag, 1)

            def add_residual(j, par):
                dve.wait_ge(ynorm_done, at(j + 1))
                dve.wait_ge(xres_in[par], at((j - par) * 8 + 16))
                nc.vector.tensor_tensor(xres[:, par, :], y_ps[:, :], xres[:, par, :],
                                        ALU.add).then_inc(res_done, 1)

            def abs_values(j, par):
                dve.wait_ge(silu_done, at(3 * j + 3))
                nc.vector.scalar_tensor_tensor(absv[:, par, :], prod[:, par, 0:I], -1.0, prod[:, par, 0:I],
                                               ALU.mult, ALU.max,
                                               accum_out=asum[:, par:par + 1]).then_inc(a_done, 1)

            def times_up(j, par, n, b):
                dve.wait_ge(u_done, at(3 * j + n + 1))
                dve.wait_ge(silu_done, at(3 * j + n + 1))
                if n == 0 and b == 0:
                    dve.wait_ge(a_done, at(j + 1))
                q = (3 + n) + 2 * par
                nc.vector.tensor_tensor(prod[:, par, CO[n]:CO[n] + CW[n]], gu_ps[q % 4][:, 0:CW[n]],
                                        prod[:, par, CO[n]:CO[n] + CW[n]], ALU.mult).then_inc(p_done, 1)

            def exact_path(par):
                done = [0]

                def then(ins):
                    done[0] += 1
                    ins.then_inc(exact, 1)
                    dve.wait_ge(exact, done[0])

                nc.vector.memset(eth[:, :], 0)
                then(nc.vector.memset(ebit[:, :], float(1 << 30)))
                with dve.Fori(0, 31):
                    dve.sem_clear(exact)
                    done[0] = 0
                    then(nc.vector.tensor_scalar(eadd[:, :], ebit[:, :], 1.0, None, ALU.mult))
                    then(nc.vector.tensor_tensor(ecand[:, :], eth[:, :], eadd[:, :], ALU.bitwise_or))
                    then(nc.vector.tensor_scalar(below[:, :], absv[:, par, :], ecand[:, :].bitcast(F32), None,
                                                 ALU.is_ge, ALU.add, accum_out=ecnt[:, :]))
                    then(nc.vector.tensor_scalar(eadd[:, :], ecnt[:, :], float(I - K) + 0.5, ebit[:, :],
                                                 ALU.is_gt, ALU.mult))
                    then(nc.vector.tensor_tensor(eth[:, :], eth[:, :], eadd[:, :], ALU.bitwise_or))
                    then(nc.vector.tensor_scalar(ebit[:, :], ebit[:, :], 0.5, None, ALU.mult))
                dve.sem_clear(exact)
                done[0] = 0
                eT = eth[:, :].bitcast(F32)
                then(nc.vector.tensor_scalar(below[:, :], absv[:, par, :], eT, None, ALU.is_lt, ALU.add,
                                             accum_out=ecnt[:, :]))
                then(nc.vector.tensor_scalar(ecnt[:, :], ecnt[:, :], -1.0, float(K), ALU.mult, ALU.add))
                then(nc.vector.tensor_scalar(below[:, :], absv[:, par, :], eT, None, ALU.is_equal))
                then(nc.vector.tensor_tensor_scan(below[:, :], below[:, :], below[:, :], 0.0, ALU.add, ALU.max))
                then(nc.vector.tensor_scalar(below[:, :], below[:, :], ecnt[:, :], None, ALU.is_gt))
                then(nc.vector.scalar_tensor_tensor(below[:, :], absv[:, par, :], eT, below[:, :],
                                                    ALU.is_equal, ALU.mult))
                then(nc.vector.scalar_tensor_tensor(absv[:, par, :], absv[:, par, :], eT, below[:, :],
                                                    ALU.is_gt, ALU.add))
                then(nc.vector.memset(kth[:, :], 0.5))
                dve.sem_clear(exact)

            def find_below(j, par):
                dve.wait_ge(thr_done, at(STEPS * j + j + STEPS + 1))
                nc.vector.scalar_tensor_tensor(below[:, :], absv[:, par, :], thr[:, par:par + 1],
                                               absv[:, par, :], ALU.is_le, ALU.mult).then_inc(below_done, 1)

            def find_top(j):
                dve.wait_ge(below_done, at(j + 1))
                dve.sem_inc(passed)
                nc.vector.max(top[:, :], below[:, :]).then_inc(top_done, 1)

            def find_flag(j, par):
                dve.wait_ge(counted, at(STEPS * j + j + STEPS + 1))
                nc.vector.tensor_scalar(rank[:, :], sgn[:, par:par + 1], 0.5, I / 2 - K, ALU.mult,
                                        ALU.add).then_inc(rank_done, 1)
                dve.wait_ge(rank_done, at(j + 1))
                dve.wait_ge(top_done, at(j + 1))
                nc.vector.scalar_tensor_tensor(pick[:, 0, :], iota[:, 0, :], rank[:, 0:1], top[:, :],
                                               ALU.is_equal, ALU.mult, accum_out=kth[:, :]).then_inc(pick_done, 1)
                nc.vector.scalar_tensor_tensor(pick[:, 1, :], iota[:, 1, :], rank[:, 0:1], top[:, :],
                                               ALU.is_equal, ALU.mult, accum_out=nxt[:, :]).then_inc(pick_done, 1)
                dve.wait_ge(pick_done, at(2 * j + 2))
                nc.vector.tensor_tensor(tied[:, :], kth[:, :], nxt[:, :], ALU.is_equal).then_inc(flag_done, 1)
                dve.wait_ge(flag_done, at(2 * j + 1))
                nc.vector.scalar_tensor_tensor(flag[:, 0:1], top[:, 0:1], thr[:, par:par + 1], tied[:, :],
                                               ALU.is_equal, ALU.max).then_inc(flag_done, 1)
                dve.wait_ge(flag_done, at(2 * j + 2))
                nc.vector.transpose(flagT[:, :], flag[:, :]).then_inc(flagT_done, 1)
                dve.wait_ge(flagT_done, at(j + 1))
                for q in range(4):
                    last = nc.vector.tensor_reduce(flagq[0:1, q:q + 1], flagT[32 * q:32 * q + 1, :], axis=AX.X,
                                                   op=ALU.max)
                last.then_inc(any_done, 1)
                dve.wait_ge(any_done, at(2 * j + 1))
                nc.vector.tensor_reduce(anyflag[0:1, :], flagq[0:1, :], axis=AX.X, op=ALU.max).then_inc(any_done, 1)

            def select(j, par):
                dve.wait_ge(any_done, at(2 * j + 2))
                dve.sem_inc(passed)
                flagged = dve.value_load(anyflag[0:1, 0:1], min_val=0, max_val=1)
                with dve.If(flagged > 0):
                    exact_path(par)
                nc.vector.scalar_tensor_tensor(prod[:, par, 0:I], absv[:, par, :], kth[:, 0:1],
                                               prod[:, par, 0:I], ALU.is_gt, ALU.mult).then_inc(h_done, 1)

            def step(j, par, b, prev, next_):
                static = isinstance(j, int)
                if next_ is not None:
                    x_stats(j + 1, 1 - par)
                if prev == 0:
                    find_below(j - 1, 1 - par)
                if next_ is not None:
                    x_normalise(j + 1, 1 - par)
                if prev == 0:
                    find_top(j - 1)
                if not static or j >= 2:
                    y_stats(j - 2)
                if b == 0:
                    abs_values(j, par)
                if next_ is not None:
                    split_x_lo(j + 1, 1 - par)
                if prev == 0:
                    find_flag(j - 1, 1 - par)
                    select(j - 1, 1 - par)
                if not static or j >= 2:
                    add_residual(j - 2, par)
                if b is not None:
                    times_up(j, par, 0, b)
                if b is not None:
                    times_up(j, par, 1, b)
                    times_up(j, par, 2, b)
                if prev is not None:
                    split_h_lo(j - 1)

            x_stats(0, 0)
            x_normalise(0, 0)
            split_x_lo(0, 0)
            pipeline(dve, step, lambda b: split_weights_lo(b, 0, 2 * JC),
                     lambda b: split_weights_lo(b, 2 * JC, JC))
            y_stats(T2 - 1)
            add_residual(T2 - 1, 1)

        @block.gpsimd
        def _(pool):
            ident_z = nc.gpsimd.memset(ident[:, :], 0.0)
            ident_z.then_inc(pool_step, 1)
            pool.wait_ge(pool_step, 1)
            nc.gpsimd.affine_select(out=ident[:, :], in_=ident[:, :], compare_op=ALU.not_equal, fill=1.0,
                                    base=0, pattern=[[-1, P]], channel_multiplier=1).then_inc(consts, 1)
            pool.wait_ge(consts, 2)

            def rstd(mv, r, k):
                nc.gpsimd.tensor_scalar(r[:, 0:1], mv[:, 1:2], EPS, None, ALU.add).then_inc(pool_step, 1)
                pool.wait_ge(pool_step, at(k + 1))
                return nc.gpsimd.tensor_tensor(r[:, 1:2], r[:, 0:1], half[:, :], ALU.pow)

            def x_rstd(j, k):
                pool.wait_ge(xag, at(j + 1))
                pool.sem_inc(passed)
                rstd(xmv, xrstd, k).then_inc(xr_done, 1)

            def y_rstd(j, k):
                pool.wait_ge(yag, at(j + 1))
                if not isinstance(j, int) or j >= 1:
                    pool.wait_ge(ynorm_done, at(j))
                pool.sem_inc(passed)
                rstd(ymv, yrstd, k).then_inc(pool_step, 1)
                pool.wait_ge(pool_step, at(k + 2))
                pool.sem_inc(passed)
                nc.gpsimd.tensor_scalar(ymean[:, :], ymv[:, 0:1], -1.0, None, ALU.mult).then_inc(pool_step, 1)
                pool.wait_ge(pool_step, at(k + 3))
                nc.gpsimd.tensor_tensor(ybias[:, :], ymean[:, :], yrstd[:, 1:2], ALU.mult).then_inc(pool_step, 1)
                pool.wait_ge(pool_step, at(k + 4))
                pool.sem_inc(passed)
                nc.gpsimd.tensor_copy(yrstd[:, 0:1], yrstd[:, 1:2]).then_inc(yr_done, 1)

            def first_guess(j, par):
                pool.wait_ge(a_done, at(j + 1))
                pool.sem_inc(passed)
                nc.gpsimd.tensor_scalar(unit[:, :], gains[:, :], asum[:, par:par + 1],
                                        1.0 / (2 * I * I * DENSITY), ALU.mult, ALU.mult)
                nc.gpsimd.tensor_scalar(thr[:, par:par + 1], asum[:, par:par + 1], GUESS / I, None,
                                        ALU.mult).then_inc(thr_done, 1)

            def newton(j, par, n, k):
                pool.wait_ge(counted, at(STEPS * j + j + n + 1))
                pool.wait_ge(thr_done, at(STEPS * j + j + n + 1))
                pool.sem_inc(passed)
                nc.gpsimd.tensor_scalar(err[:, :], sgn[:, par:par + 1], -1.0, float(2 * AIM - I),
                                        ALU.mult, ALU.add).then_inc(pool_step, 1)
                pool.wait_ge(pool_step, at(k + 1))
                pool.sem_inc(passed)
                nc.gpsimd.tensor_scalar(move[:, :], err[:, :], err[:, :], float((WINDOW - 1) ** 2) + 0.5,
                                        ALU.mult, ALU.is_gt).then_inc(pool_step, 1)
                pool.wait_ge(pool_step, at(k + 2))
                nc.gpsimd.tensor_tensor(delta[:, :], err[:, :], move[:, :], ALU.mult).then_inc(pool_step, 1)
                pool.wait_ge(pool_step, at(k + 3))
                pool.sem_inc(passed)
                nc.gpsimd.tensor_scalar(thr[:, par:par + 1], delta[:, :], unit[:, n:n + 1],
                                        thr[:, par:par + 1], ALU.mult, ALU.add).then_inc(thr_done, 1)

            XK, YK, NK = 1, 4, 3

            def step(j, par, b, prev, next_):
                static = isinstance(j, int)
                k = (1 + XK * (min(j + 1, T2) if static else j + 1) + YK * (max(j - 2, 0) if static else j - 2)
                     + NK * STEPS * (j if b == 0 else TILES))
                if next_ is not None:
                    x_rstd(j + 1, k)
                    k = k + XK
                if not static or j >= 2:
                    y_rstd(j - 2, k)
                    k = k + YK
                if b == 0:
                    first_guess(j, par)
                    for n in range(STEPS):
                        newton(j, par, n, k)
                        k = k + NK

            x_rstd(0, 1)
            pipeline(pool, step)
            y_rstd(T2 - 1, 1 + XK * T2 + YK * (T2 - 1) + NK * STEPS * TILES)


CONSTS = 2

_INS = ["L0_attn_x", "L0_attn_w_gate", "L0_attn_w_up", "L0_attn_w_down",
        "L0_ffn_W_gate", "L0_ffn_W_up", "L0_ffn_W_down"]


def kernel(**inputs):
    import concourse.bacc as _bacc
    from concourse.bass_utils import run_bass_kernel_spmd as _run

    nc = _bacc.Bacc("TRN2", target_bir_lowering=False, num_devices=1)
    arrays, args = {}, []
    for name in _INS:
        a = np.ascontiguousarray(inputs[name])
        arrays[f"in_{name}"] = a
        args.append(nc.dram_tensor(f"in_{name}", a.shape, mybir.dt.from_np(a.dtype), kind="ExternalInput").ap())
    shape = inputs["L0_attn_x"].shape
    args.append(nc.dram_tensor("out_0", shape, F32, kind="ExternalOutput").ap())
    sandwich(nc, *args)
    r = _run(nc, [arrays], core_ids=[0])
    return r.results[0]["out_0"]
```

```python
import numpy as np
import concourse.bass as bass
from concourse import mybir
from contextlib import ExitStack

F32 = mybir.dt.float32
F32R = mybir.dt.float32r
BF16 = mybir.dt.bfloat16
I32 = mybir.dt.int32
ALU = mybir.AluOpType
ACT = mybir.ActivationFunctionType
AX = mybir.AxisListType

P = 128


class Tile:

    def __init__(self, i, m, c):
        self.i, self.m, self.c = i, m, c

    def __add__(self, n):
        return Tile(self.i, self.m + n.m, self.c + n.c) if isinstance(n, Tile) else Tile(self.i, self.m, self.c + n)

    def __sub__(self, n):
        return Tile(self.i, self.m, self.c - n)

    def __mul__(self, n):
        return Tile(self.i, self.m * n, self.c * n)

    __radd__, __rmul__ = __add__, __mul__


def at(n):
    return n.i * n.m + n.c if isinstance(n, Tile) else n


def sandwich(nc, x, w_gate, w_up, w_down, W_gate, W_up, W_down, out):
    B, S, H = x.shape
    I = w_gate.shape[0]
    TOK = B * S
    TILES = TOK // P
    KC = H // P
    JC = -(-I // P)
    LASTJ = I - (JC - 1) * P
    IP = JC * P
    CW = [460, 460, 456]
    CO = [0, 460, 920]
    TG = [(0, 4), (4, 4), (8, 3)]
    assert sum(CW) == I and H == 512 and TOK % (2 * P) == 0 and I == 1376
    EPS = 1e-5

    K = I // 2
    WINDOW = 8
    AIM = K + (WINDOW - 1) / 2
    GUESS, DENSITY = 0.79, 0.63
    GAIN = [1.0, 1.0, 0.7, 0.5, 0.7]
    STEPS = len(GAIN)

    xf = x.rearrange("b s h -> (b s) h")
    of = out.rearrange("b s h -> (b s) h")
    x1 = nc.dram_tensor("x1_scratch", (TOK, H), F32, kind="Internal").ap()
    weights = [(w_gate, w_up, w_down), (W_gate, W_up, W_down)]

    ctx = ExitStack()
    with ctx:
        def sb(name, shape, dt=F32):
            return ctx.enter_context(nc.sbuf_tensor(name, shape, dt))

        def sem(name):
            return ctx.enter_context(nc.semaphore(name))

        gu_hi = [sb(n, [P, KC, I], F32R) for n in ("gate_hi", "up_hi")]
        gu_lo = [sb(n, [P, KC, I], F32R) for n in ("gate_lo", "up_lo")]
        down_hi = sb("down_hi", [P, JC, H], F32R)
        down_lo = sb("down_lo", [P, JC, H], F32R)
        NSTAGE = 7
        stage = sb("stage", [P, NSTAGE, H])
        ident = sb("ident", [P, P])
        xin = sb("xin", [P, 2, H])
        xres = sb("xres", [P, 2, H])
        xT_hi = [sb(f"xT_hi{i}", [P, KC, P], F32R) for i in range(2)]
        xT_lo = [sb(f"xT_lo{i}", [P, KC, P], F32R) for i in range(2)]
        absv = sb("absv", [P, 2, I])
        prod = sb("prod", [P, 2, IP])
        below = sb("below", [P, I])
        junk = sb("junk", [P, I], BF16)
        hT_hi = sb("hT_hi", [P, JC, P], F32R)
        hT_lo = sb("hT_lo", [P, JC, P], F32R)

        xstat = sb("xstat", [P, 6])
        xmv = sb("xmv", [P, 2])
        xrstd = sb("xrstd", [P, 2])
        ystat = sb("ystat", [P, 6])
        ymv = sb("ymv", [P, 2])
        yrstd = sb("yrstd", [P, 2])
        ybias = sb("ybias", [P, 1])
        half = sb("half", [P, 1])
        asum = sb("asum", [P, 2])
        gains = sb("gains", [P, STEPS])
        unit = sb("unit", [P, STEPS])
        thr = sb("thr", [P, 2])
        sgn = sb("sgn", [P, 2])
        err = sb("err", [P, 1])
        ymean = sb("ymean", [P, 1])
        move = sb("move", [P, 1])
        delta = sb("delta", [P, 1])
        rank = sb("rank", [P, 1])
        tied = sb("tied", [P, 1])
        top = sb("top", [P, 8])
        iota = sb("iota", [P, 2, 8])
        pick = sb("pick", [P, 2, 8])
        kth = sb("kth", [P, 1])
        nxt = sb("nxt", [P, 1])
        flag = sb("flag", [P, 32])
        flagT = sb("flagT", [P, 32])
        flagq = sb("flagq", [P, 4])
        anyflag = sb("anyflag", [P, 1], I32)
        ebit = sb("ebit", [P, 1])
        ecnt = sb("ecnt", [P, 1])
        eadd = sb("eadd", [P, 1], I32)
        ecand = sb("ecand", [P, 1], I32)
        eth = sb("eth", [P, 1], I32)

        gu_ps = [ctx.enter_context(nc.psum_tensor(f"gu_ps{i}", [P, 512], F32)) for i in range(4)]
        tr_ps = [ctx.enter_context(nc.psum_tensor(f"tr_ps{i}", [P, 4, P], F32)) for i in range(3)]
        y_ps = ctx.enter_context(nc.psum_tensor("y_ps", [P, H], F32))

        def y_bank(j):
            return gu_ps[0] if isinstance(j, int) and j == 2 * TILES - 1 else y_ps

        stage_in = [sem(f"stage_in{i}") for i in range(NSTAGE)]
        w_tr, whi_done, wlo_done = sem("w_tr"), sem("whi_done"), sem("wlo_done")
        x_in = [sem(f"x_in{i}") for i in range(2)]
        xres_in = [sem(f"xres_in{i}") for i in range(2)]
        stored = [sem(f"stored{i}") for i in range(2)]
        consts = sem("consts")
        g_done, u_done, x_tr, h_tr, y_done = map(sem, ("g_done", "u_done", "x_tr", "h_tr", "y_done"))
        silu_done, xhi_done, hhi_done, ynorm_done, counted = map(
            sem, ("silu_done", "xhi_done", "hhi_done", "ynorm_done", "counted"))
        a_done, p_done, xn_done, xlo_done, hlo_done, res_done = map(
            sem, ("a_done", "p_done", "xn_done", "xlo_done", "hlo_done", "res_done"))
        xst, xag, yst, yag = map(sem, ("xst", "xag", "yst", "yag"))
        below_done, top_done, rank_done, pick_done, flag_done, flagT_done, any_done, h_done = map(
            sem, ("below_done", "top_done", "rank_done", "pick_done", "flag_done", "flagT_done",
                  "any_done", "h_done"))
        xr_done, yr_done, thr_done, pool_step = map(sem, ("xr_done", "yr_done", "thr_done", "pool_step"))
        exact = sem("exact")
        passed = sem("passed")

        block = ctx.enter_context(nc.Block())

        T2 = 2 * TILES

        PREP = {
            "pe": {0: {"G0": (4, 8), "G1": (8, 11), "G2": (11, 15), "U0": (15, 19), "U1": (19, 22),
                       "U2": (22, 25), "N": (25, 28)},
                   1: {"G1": (28, 30), "G2": (30, 32), "U1": (32, 33)},
                   15: {"U1": (33, 35), "D1": (35, 38), "D2": (38, 41), "end": (41, 43)},
                   16: {"G1": (43, 46), "G2": (46, 48), "X": (48, 51), "U1": (51, 55)},
                   17: {"G1": (55, 58), "G2": (58, 61), "U0": (61, 62), "U1": (62, 64), "U2": (64, 66)}},
            "act": {0: {"G0": (4, 8), "G1": (8, 11), "G2": (11, 15), "C0": (15, 19), "C1": (19, 22),
                        "C2": (22, 24), "C3": (24, 26), "C4": (26, 28), "C5": (28, 30)},
                    1: {"G2": (30, 32), "C0": (32, 33)},
                    15: {"Y": (33, 35), "C2": (35, 38), "C3": (38, 40), "C4": (40, 41), "C5": (41, 43)},
                    16: {"G1": (43, 46), "G2": (46, 48), "X": (48, 51), "Y": (51, 55)},
                    17: {"G1": (55, 58), "G2": (58, 61), "H": (61, 66)}},
            "dve": {0: {"X": (4, 8), "A": (8, 15), "U0": (15, 19), "U1": (19, 22), "U2": (22, 24),
                        "end": (24, 30)},
                    1: {"A": (30, 32), "U0": (32, 33)},
                    15: {"F": (33, 35), "end": (35, 43)},
                    16: {"X": (43, 46), "B": (46, 48), "A": (48, 51), "F": (51, 55)},
                    17: {"X": (55, 58), "A": (58, 61), "U0": (61, 62), "U1": (62, 64), "U2": (64, 66)}},
        }
        CHUNKS = [-(-(CO[n] + CW[n]) // P) for n in range(3)]

        def prepare(engine, chunk, j, place):
            if isinstance(j, int):
                for w in range(*PREP[engine].get(j, {}).get(place, (0, 0))):
                    chunk(w)

        def pipeline(eng, step):
            for b in range(2):
                j0 = b * TILES
                step(j0, 0, b, prev=b - 1 if b else None, next_=b)
                step(j0 + 1, 1, b, prev=b, next_=b)
                step(j0 + 2, 0, b, prev=b, next_=b)
                with eng.Fori(0, (TILES - 4) // 2) as i:
                    j = Tile(i, 2, j0 + 3)
                    step(j, 1, b, prev=b, next_=b)
                    step(j + 1, 0, b, prev=b, next_=b)
                step(j0 + TILES - 1, 1, b, prev=b, next_=b + 1 if b == 0 else None)
            step(T2, 0, None, prev=1, next_=None)

        def weight_chunk(w):
            b, n = divmod(w, 3 * JC)
            m, c = divmod(n, JC)
            return b, m, c, P if c < JC - 1 else LASTJ

        @block.sync
        def _(sp):
            def rows(t, j, b):
                return t[bass.ds(at((j - b * TILES) * P), P), :]

            def load_x(j, par, b):
                if not isinstance(j, int) or j >= 2:
                    sp.wait_ge(x_tr, at(j - 1))
                if b == 1:
                    sp.wait_ge(stored[par], at((j - TILES - par) * 8 + 16))
                sp.dma_start(xin[:, par, :], rows(xf if b == 0 else x1, j, b)).then_inc(x_in[par], 16)

            def load_w(w):
                b, m, c, size = weight_chunk(w)
                slot = w % NSTAGE
                if w >= NSTAGE:
                    sp.wait_ge(w_tr, w - NSTAGE + 1)
                if m < 2:
                    src, dst = weights[b][m][c * P:c * P + size, :], stage[0:size, slot, :]
                else:
                    src = weights[b][2][:, c * P:c * P + size].rearrange("(r p) q -> p r q", p=P)
                    dst = stage[:, slot, :].rearrange("p (r q) -> p r q", q=P)[:, :, 0:size]
                sp.dma_start(dst, src).then_inc(stage_in[slot], 16)

            def store(j, par, b):
                sp.wait_ge(res_done, at(j + 1))
                sp.dma_start(rows(x1 if b == 0 else of, j, b), xres[:, par, :]).then_inc(stored[par], 16)

            def load_res(j, par, b):
                if not isinstance(j, int) or j >= 2:
                    sp.wait_ge(stored[par], at((j - par) * 8))
                sp.dma_start(xres[:, par, :], rows(xf if b == 0 else x1, j, b)).then_inc(xres_in[par], 16)

            def step(j, par, b, prev, next_, ahead=True):
                if next_ is not None and ahead:
                    load_x(j + 1, 1 - par, next_)
                if not isinstance(j, int):
                    store(j - 2, par, b)
                elif j >= 2:
                    store(j - 2, par, (j - 2) // TILES)
                if prev is not None:
                    load_res(j - 1, 1 - par, prev)

            load_x(0, 0, 0)
            for w in range(4):
                load_w(w)
            load_x(1, 1, 0)
            for w in range(4, 3 * JC):
                load_w(w)
            step(1, 1, 0, 0, 0)
            step(2, 0, 0, 0, 0)
            with sp.Fori(0, (TILES - 4) // 2) as i:
                j = Tile(i, 2, 3)
                step(j, 1, 0, 0, 0)
                step(j + 1, 0, 0, 0, 0)
            load_x(TILES, 0, 1)
            load_x(TILES + 1, 1, 1)
            for w in range(3 * JC, 3 * JC + NSTAGE):
                load_w(w)
            step(TILES - 1, 1, 0, 0, 1, ahead=False)
            for w in range(3 * JC + NSTAGE, 5 * JC):
                load_w(w)
            step(TILES, 0, 1, 0, 1, ahead=False)
            load_x(TILES + 2, 0, 1)
            for w in range(5 * JC, 6 * JC):
                load_w(w)
            step(TILES + 1, 1, 1, 1, 1, ahead=False)
            step(TILES + 2, 0, 1, 1, 1)
            with sp.Fori(0, (TILES - 4) // 2) as i:
                j = Tile(i, 2, TILES + 3)
                step(j, 1, 1, 1, 1)
                step(j + 1, 0, 1, 1, 1)
            step(T2 - 1, 1, 1, 1, None)
            step(T2, 0, 1, 1, None)
            store(T2 - 1, 1, 1)
            for i in range(2):
                sp.wait_ge(stored[i], 16 * TILES)

        @block.tensor
        def _(pe):
            sent = {"x": 0, "h": 0, "w": 0}

            def transpose_weights(w):
                b, m, c, size = weight_chunk(w)
                slot = w % NSTAGE
                pe.wait_ge(stage_in[slot], 16 * (w // NSTAGE + 1))
                if w >= 3:
                    pe.wait_ge(wlo_done, w - 2)
                if w % 3 == 2 and sent["x"]:
                    pe.wait_ge(xlo_done, sent["x"])
                if sent["h"]:
                    pe.wait_ge(hlo_done, 3 * (sent["h"] - 1) + w % 3 + 1)
                for r in range(KC):
                    if m < 2:
                        last = nc.tensor.transpose(tr_ps[w % 3][:, r, 0:size],
                                                   stage[0:size, slot, r * P:(r + 1) * P],
                                                   ident[0:size, 0:size])
                    else:
                        last = nc.tensor.transpose(tr_ps[w % 3][0:size, r, :],
                                                   stage[:, slot, r * P:r * P + size], ident[:, :])
                last.then_inc(w_tr, 1)
                sent["w"] = w + 1

            def bank_free_of_weights(j, bank):
                if isinstance(j, int) and sent["w"] > bank:
                    pe.wait_ge(wlo_done, (sent["w"] - 1 - bank) // 3 * 3 + bank + 1)

            def transpose_x(j, par, wait_h):
                pe.wait_ge(xn_done, at(j + 1))
                bank_free_of_weights(j, 2)
                if wait_h is not None:
                    pe.wait_ge(hlo_done, at(wait_h))
                for c in range(KC):
                    last = nc.tensor.transpose(tr_ps[2][:, c, :], xin[:, par, c * P:(c + 1) * P], ident[:, :])
                last.then_inc(x_tr, 1)
                if isinstance(j, int):
                    sent["x"] = j + 1

            def product(j, par, m, n):
                q = (3 * m + n) + 2 * par
                bank = gu_ps[q % 4]
                first = isinstance(j, int) and j == 0
                if (m, n) == (0, 0) and not first:
                    pe.wait_ge(silu_done, at(3 * j))
                elif m == 0 and not first:
                    pe.wait_ge(p_done, at(3 * j - 3 + n))
                elif (m, n) == (1, 0) and not first:
                    pe.wait_ge(p_done, at(3 * j))
                elif m == 1 and n > 0:
                    pe.wait_ge(silu_done, at(3 * j + n))
                if isinstance(j, int) and j % TILES == 0:
                    pe.wait_ge(wlo_done, (3 * (j // TILES) + m) * JC + CHUNKS[n])
                cols = slice(CO[n], CO[n] + CW[n])
                for c in range(KC):
                    for i, (xt, w) in enumerate(((xT_hi, gu_lo), (xT_lo, gu_hi), (xT_hi, gu_hi))):
                        last = nc.tensor.matmul(bank[:, 0:CW[n]], xt[par][:, c, :], w[m][:, c, cols],
                                                start=(c == 0 and i == 0), stop=(c == KC - 1 and i == 2))
                last.then_inc((g_done, u_done)[m], 1)

            def transpose_h(j, par, blk, x_next):
                if blk == 0:
                    pe.wait_ge(h_done, at(j + 1))
                else:
                    pe.wait_ge(p_done, at(3 * j + 3))
                for g, (c0, cn) in enumerate(TG):
                    bank_free_of_weights(j, g)
                    if g == 2 and x_next:
                        pe.wait_ge(xlo_done, at(j + 3))
                    for c in range(cn):
                        last = nc.tensor.transpose(tr_ps[g][:, c, :],
                                                   prod[:, par, (c0 + c) * P:(c0 + c + 1) * P], ident[:, :])
                    last.then_inc(h_tr, 1)
                if isinstance(j, int):
                    sent["h"] = j + 1

            def down(j):
                if isinstance(j, int) and j == T2 - 1:
                    pe.wait_ge(silu_done, 3 * T2)
                elif not isinstance(j, int) or j >= 1:
                    pe.wait_ge(res_done, at(j))
                if isinstance(j, int) and j % TILES == 0:
                    pe.wait_ge(wlo_done, 3 * JC * (j // TILES + 1))
                for g, (c0, cn) in enumerate(TG):
                    prepare("pe", transpose_weights, j + 1, f"D{g}")
                    pe.wait_ge(hlo_done, at(3 * j + g + 1))
                    for c in range(c0, c0 + cn):
                        k = P if c < JC - 1 else LASTJ
                        for i, (h, w) in enumerate(((hT_hi, down_lo), (hT_lo, down_hi), (hT_hi, down_hi))):
                            last = nc.tensor.matmul(y_bank(j)[:, :], h[0:k, c, :], w[0:k, c, :],
                                                    start=(c == 0 and i == 0),
                                                    stop=(c == JC - 1 and i == 2))
                last.then_inc(y_done, 1)

            def step(j, par, b, prev, next_):
                static = isinstance(j, int)
                def weights_at(place):
                    prepare("pe", transpose_weights, j, place)

                x_at = 1 if static and j == TILES else 0
                if b is not None:
                    if static and j % TILES == 0:
                        pe.wait_ge(xlo_done, at(j + 1))
                        weights_at("G0")
                        product(j, par, 0, 0)
                    for n in (1, 2):
                        weights_at(f"G{n}")
                        product(j, par, 0, n)
                    weights_at("X")
                    for n in range(3):
                        if n == x_at and next_ is not None:
                            transpose_x(j + 1, 1 - par, None if static and j < 2 else 3 * (j - 1))
                        weights_at(f"U{n}")
                        product(j, par, 1, n)
                if prev is not None:
                    if not static or j >= 2:
                        pe.wait_ge(hlo_done, at(3 * (j - 1)))
                    transpose_h(j - 1, 1 - par, prev, next_ is not None)
                weights_at("N")
                if next_ is not None and next_ == b:
                    pe.wait_ge(xlo_done, at(j + 2))
                    product(j + 1, 1 - par, 0, 0)
                if prev is not None:
                    down(j - 1)
                weights_at("end")

            pe.wait_ge(consts, CONSTS)
            for w in range(3):
                transpose_weights(w)
            transpose_x(0, 0, None)
            transpose_weights(3)
            pipeline(pe, step)

        @block.scalar
        def _(act):
            def split_weights_hi(w):
                b, m, c, size = weight_chunk(w)
                if b == 1 and c == 0:
                    act.wait_ge((g_done, u_done, y_done)[m], TILES * (3 if m < 2 else 1))
                act.wait_ge(w_tr, w + 1)
                if m < 2:
                    src, dst = tr_ps[w % 3][:, :, 0:size], gu_hi[m][:, :, c * P:c * P + size]
                else:
                    src = tr_ps[w % 3][0:size, :, :].rearrange("q r p -> q (r p)")
                    dst = down_hi[0:size, c, :]
                nc.scalar.activation(dst, src, ACT.Copy).then_inc(whi_done, 1)

            def count(j, par, n):
                act.wait_ge(thr_done, at(STEPS * j + j + n + 1))
                nc.scalar.activation(junk[:, :], absv[:, par, :], ACT.Sign, bias=thr[:, par:par + 1],
                                     scale=-1.0, accum_out=sgn[:, par:par + 1]).then_inc(counted, 1)

            def silu(j, par, n):
                act.wait_ge(g_done, at(3 * j + n + 1))
                if n == 0 and (not isinstance(j, int) or j >= 2):
                    act.wait_ge(h_tr, at(3 * (j - 1)))
                q = n + 2 * par
                nc.scalar.activation(prod[:, par, CO[n]:CO[n] + CW[n]], gu_ps[q % 4][:, 0:CW[n]],
                                     ACT.Silu).then_inc(silu_done, 1)

            def split_x_hi(j, par):
                act.wait_ge(x_tr, at(j + 1))
                if not isinstance(j, int) or j >= 2:
                    act.wait_ge(u_done, at(3 * (j - 1)))
                nc.scalar.activation(xT_hi[par][:, :, :], tr_ps[2][:, :, :], ACT.Copy).then_inc(xhi_done, 1)

            def split_h_hi(j):
                for g, (c0, cn) in enumerate(TG):
                    act.wait_ge(h_tr, at(3 * j + g + 1))
                    if g == 0 and (not isinstance(j, int) or j >= 1):
                        act.wait_ge(y_done, at(j))
                    nc.scalar.activation(hT_hi[:, c0:c0 + cn, :], tr_ps[g][:, 0:cn, :],
                                         ACT.Copy).then_inc(hhi_done, 1)

            def normalise_y(j):
                act.wait_ge(yr_done, at(j + 1))
                nc.scalar.activation(y_bank(j)[:, :], y_bank(j)[:, :], ACT.Identity, bias=ybias[:, 0:1],
                                     scale=yrstd[:, 0:1]).then_inc(ynorm_done, 1)

            def step(j, par, b, prev, next_):
                static = isinstance(j, int)

                def weights_at(place):
                    prepare("act", split_weights_hi, j, place)

                if b is not None:
                    if static and j % TILES == 0:
                        weights_at("G0")
                        silu(j, par, 0)
                    for n in (1, 2):
                        weights_at(f"G{n}")
                        silu(j, par, n)
                weights_at("X")
                if next_ is not None:
                    split_x_hi(j + 1, 1 - par)
                weights_at("Y")
                if not (static and j == T2) and (not static or j >= 2):
                    normalise_y(j - 2)
                if b == 0:
                    weights_at("C0")
                    count(j, par, 0)
                weights_at("H")
                if prev is not None:
                    split_h_hi(j - 1)
                if static and j == T2:
                    normalise_y(j - 2)
                if b == 0:
                    weights_at("C1")
                    count(j, par, 1)
                if next_ is not None and next_ == b and not (static and j == 0):
                    silu(j + 1, 1 - par, 0)
                if b == 0:
                    for n in range(2, STEPS + 1):
                        weights_at(f"C{n}")
                        count(j, par, n)
                if static and j == 0:
                    silu(1, 1, 0)
                weights_at("end")

            for w in range(3):
                split_weights_hi(w)
            split_x_hi(0, 0)
            split_weights_hi(3)
            pipeline(act, step)
            normalise_y(T2 - 1)

        @block.vector
        def _(dve):
            for n in range(8):
                nc.vector.memset(iota[:, 0, n:n + 1], float(n))
                nc.vector.memset(iota[:, 1, n:n + 1], float(n + 1) if n < 7 else -1e6)
            for n, g in enumerate(GAIN):
                nc.vector.memset(gains[:, n:n + 1], g)
            nc.vector.memset(flag[:, :], 0.0)
            nc.vector.memset(prod[:, :, I:IP], 0.0)
            nc.vector.memset(half[:, :], -0.5).then_inc(consts, 1)
            dve.wait_ge(consts, CONSTS)

            def split_weights_lo(w):
                b, m, c, size = weight_chunk(w)
                dve.wait_ge(whi_done, w + 1)
                if m < 2:
                    src, cols = tr_ps[w % 3][:, :, 0:size], slice(c * P, c * P + size)
                    hi, lo = gu_hi[m][:, :, cols], gu_lo[m][:, :, cols]
                else:
                    src = tr_ps[w % 3][0:size, :, :].rearrange("q r p -> q (r p)")
                    hi, lo = down_hi[0:size, c, :], down_lo[0:size, c, :]
                nc.vector.tensor_tensor(lo, src, hi.bitcast(F32), ALU.subtract).then_inc(wlo_done, 1)

            def x_stats(j, par):
                dve.wait_ge(x_in[par], at((j - par) * 8 + 16))
                if not isinstance(j, int) or j >= 1:
                    dve.wait_ge(xn_done, at(j))
                nc.vector.bn_stats(xstat[:, :], xin[:, par, :]).then_inc(xst, 1)
                dve.wait_ge(xst, at(j + 1))
                dve.sem_inc(passed)
                nc.vector.bn_aggr(xmv[:, :], xstat[:, :]).then_inc(xag, 1)

            def x_normalise(j, par):
                dve.wait_ge(xr_done, at(j + 1))
                nc.vector.tensor_scalar(xin[:, par, :], xin[:, par, :], xmv[:, 0:1], xrstd[:, 1:2],
                                        ALU.subtract, ALU.mult).then_inc(xn_done, 1)

            def split_x_lo(j, par):
                dve.wait_ge(xhi_done, at(j + 1))
                nc.vector.tensor_tensor(xT_lo[par][:, :, :], tr_ps[2][:, :, :],
                                        xT_hi[par][:, :, :].bitcast(F32), ALU.subtract).then_inc(xlo_done, 1)

            def split_h_lo(j):
                for g, (c0, cn) in enumerate(TG):
                    dve.wait_ge(hhi_done, at(3 * j + g + 1))
                    nc.vector.tensor_tensor(hT_lo[:, c0:c0 + cn, :], tr_ps[g][:, 0:cn, :],
                                            hT_hi[:, c0:c0 + cn, :].bitcast(F32),
                                            ALU.subtract).then_inc(hlo_done, 1)

            def y_stats(j):
                dve.wait_ge(y_done, at(j + 1))
                nc.vector.bn_stats(ystat[:, :], y_bank(j)[:, :]).then_inc(yst, 1)
                dve.wait_ge(yst, at(j + 1))
                dve.sem_inc(passed)
                nc.vector.bn_aggr(ymv[:, :], ystat[:, :]).then_inc(yag, 1)

            def add_residual(j, par):
                dve.wait_ge(ynorm_done, at(j + 1))
                dve.wait_ge(xres_in[par], at((j - par) * 8 + 16))
                nc.vector.tensor_tensor(xres[:, par, :], y_bank(j)[:, :], xres[:, par, :],
                                        ALU.add).then_inc(res_done, 1)

            def abs_values(j, par):
                dve.wait_ge(silu_done, at(3 * j + 3))
                nc.vector.scalar_tensor_tensor(absv[:, par, :], prod[:, par, 0:I], -1.0, prod[:, par, 0:I],
                                               ALU.mult, ALU.max,
                                               accum_out=asum[:, par:par + 1]).then_inc(a_done, 1)

            def times_up(j, par, n, b):
                dve.wait_ge(u_done, at(3 * j + n + 1))
                dve.wait_ge(silu_done, at(3 * j + n + 1))
                if n == 0 and b == 0:
                    dve.wait_ge(a_done, at(j + 1))
                q = (3 + n) + 2 * par
                nc.vector.tensor_tensor(prod[:, par, CO[n]:CO[n] + CW[n]], gu_ps[q % 4][:, 0:CW[n]],
                                        prod[:, par, CO[n]:CO[n] + CW[n]], ALU.mult).then_inc(p_done, 1)

            def exact_path(par):
                done = [0]

                def then(ins):
                    done[0] += 1
                    ins.then_inc(exact, 1)
                    dve.wait_ge(exact, done[0])

                nc.vector.memset(eth[:, :], 0)
                then(nc.vector.memset(ebit[:, :], float(1 << 30)))
                with dve.Fori(0, 31):
                    dve.sem_clear(exact)
                    done[0] = 0
                    then(nc.vector.tensor_scalar(eadd[:, :], ebit[:, :], 1.0, None, ALU.mult))
                    then(nc.vector.tensor_tensor(ecand[:, :], eth[:, :], eadd[:, :], ALU.bitwise_or))
                    then(nc.vector.tensor_scalar(below[:, :], absv[:, par, :], ecand[:, :].bitcast(F32), None,
                                                 ALU.is_ge, ALU.add, accum_out=ecnt[:, :]))
                    then(nc.vector.tensor_scalar(eadd[:, :], ecnt[:, :], float(I - K) + 0.5, ebit[:, :],
                                                 ALU.is_gt, ALU.mult))
                    then(nc.vector.tensor_tensor(eth[:, :], eth[:, :], eadd[:, :], ALU.bitwise_or))
                    then(nc.vector.tensor_scalar(ebit[:, :], ebit[:, :], 0.5, None, ALU.mult))
                dve.sem_clear(exact)
                done[0] = 0
                eT = eth[:, :].bitcast(F32)
                then(nc.vector.tensor_scalar(below[:, :], absv[:, par, :], eT, None, ALU.is_lt, ALU.add,
                                             accum_out=ecnt[:, :]))
                then(nc.vector.tensor_scalar(ecnt[:, :], ecnt[:, :], -1.0, float(K), ALU.mult, ALU.add))
                then(nc.vector.tensor_scalar(below[:, :], absv[:, par, :], eT, None, ALU.is_equal))
                then(nc.vector.tensor_tensor_scan(below[:, :], below[:, :], below[:, :], 0.0, ALU.add, ALU.max))
                then(nc.vector.tensor_scalar(below[:, :], below[:, :], ecnt[:, :], None, ALU.is_gt))
                then(nc.vector.scalar_tensor_tensor(below[:, :], absv[:, par, :], eT, below[:, :],
                                                    ALU.is_equal, ALU.mult))
                then(nc.vector.scalar_tensor_tensor(absv[:, par, :], absv[:, par, :], eT, below[:, :],
                                                    ALU.is_gt, ALU.add))
                then(nc.vector.memset(kth[:, :], 0.5))
                dve.sem_clear(exact)

            def find_below(j, par):
                dve.wait_ge(thr_done, at(STEPS * j + j + STEPS + 1))
                nc.vector.scalar_tensor_tensor(below[:, :], absv[:, par, :], thr[:, par:par + 1],
                                               absv[:, par, :], ALU.is_le, ALU.mult).then_inc(below_done, 1)

            def find_top(j):
                dve.wait_ge(below_done, at(j + 1))
                dve.sem_inc(passed)
                nc.vector.max(top[:, :], below[:, :]).then_inc(top_done, 1)

            def find_flag(j, par):
                dve.wait_ge(counted, at(STEPS * j + j + STEPS + 1))
                nc.vector.tensor_scalar(rank[:, :], sgn[:, par:par + 1], 0.5, I / 2 - K, ALU.mult,
                                        ALU.add).then_inc(rank_done, 1)
                dve.wait_ge(rank_done, at(j + 1))
                dve.wait_ge(top_done, at(j + 1))
                nc.vector.scalar_tensor_tensor(pick[:, 0, :], iota[:, 0, :], rank[:, 0:1], top[:, :],
                                               ALU.is_equal, ALU.mult, accum_out=kth[:, :]).then_inc(pick_done, 1)
                nc.vector.scalar_tensor_tensor(pick[:, 1, :], iota[:, 1, :], rank[:, 0:1], top[:, :],
                                               ALU.is_equal, ALU.mult, accum_out=nxt[:, :]).then_inc(pick_done, 1)
                dve.wait_ge(pick_done, at(2 * j + 2))
                nc.vector.tensor_tensor(tied[:, :], kth[:, :], nxt[:, :], ALU.is_equal).then_inc(flag_done, 1)
                dve.wait_ge(flag_done, at(2 * j + 1))
                nc.vector.scalar_tensor_tensor(flag[:, 0:1], top[:, 0:1], thr[:, par:par + 1], tied[:, :],
                                               ALU.is_equal, ALU.max).then_inc(flag_done, 1)
                dve.wait_ge(flag_done, at(2 * j + 2))
                nc.vector.transpose(flagT[:, :], flag[:, :]).then_inc(flagT_done, 1)
                dve.wait_ge(flagT_done, at(j + 1))
                for q in range(4):
                    last = nc.vector.tensor_reduce(flagq[0:1, q:q + 1], flagT[32 * q:32 * q + 1, :], axis=AX.X,
                                                   op=ALU.max)
                last.then_inc(any_done, 1)
                dve.wait_ge(any_done, at(2 * j + 1))
                nc.vector.tensor_reduce(anyflag[0:1, :], flagq[0:1, :], axis=AX.X, op=ALU.max).then_inc(any_done, 1)

            def select(j, par):
                dve.wait_ge(any_done, at(2 * j + 2))
                dve.sem_inc(passed)
                flagged = dve.value_load(anyflag[0:1, 0:1], min_val=0, max_val=1)
                with dve.If(flagged > 0):
                    exact_path(par)
                nc.vector.scalar_tensor_tensor(prod[:, par, 0:I], absv[:, par, :], kth[:, 0:1],
                                               prod[:, par, 0:I], ALU.is_gt, ALU.mult).then_inc(h_done, 1)

            def step(j, par, b, prev, next_):
                static = isinstance(j, int)

                def weights_at(place):
                    prepare("dve", split_weights_lo, j, place)

                if next_ is not None:
                    x_stats(j + 1, 1 - par)
                weights_at("X")
                below_first = static and j in (1, TILES)
                if prev == 0 and below_first:
                    find_below(j - 1, 1 - par)
                if next_ is not None:
                    x_normalise(j + 1, 1 - par)
                if prev == 0 and not below_first:
                    find_below(j - 1, 1 - par)
                weights_at("B")
                if prev == 0:
                    find_top(j - 1)
                if not static or j >= 2:
                    y_stats(j - 2)
                weights_at("A")
                if static and j == 1:
                    split_x_lo(2, 0)
                if prev == 0:
                    find_flag(j - 1, 1 - par)
                if static and j == TILES:
                    split_x_lo(j + 1, 1)
                weights_at("F")
                if b == 0:
                    abs_values(j, par)
                if prev == 0:
                    select(j - 1, 1 - par)
                if next_ is not None and not (static and j in (1, TILES)):
                    split_x_lo(j + 1, 1 - par)
                h_lo_first = static and j in (TILES - 1, T2)
                if h_lo_first and j == T2:
                    split_h_lo(j - 1)
                if not static or j >= 2:
                    add_residual(j - 2, par)
                if h_lo_first and j < T2:
                    split_h_lo(j - 1)
                for n in range(3):
                    weights_at(f"U{n}")
                    if b is not None:
                        times_up(j, par, n, b)
                if prev is not None and not h_lo_first:
                    split_h_lo(j - 1)
                weights_at("end")

            x_stats(0, 0)
            split_weights_lo(0)
            x_normalise(0, 0)
            split_weights_lo(1)
            split_weights_lo(2)
            split_x_lo(0, 0)
            split_weights_lo(3)
            pipeline(dve, step)
            y_stats(T2 - 1)
            add_residual(T2 - 1, 1)

        @block.gpsimd
        def _(pool):
            ident_z = nc.gpsimd.memset(ident[:, :], 0.0)
            ident_z.then_inc(pool_step, 1)
            pool.wait_ge(pool_step, 1)
            nc.gpsimd.affine_select(out=ident[:, :], in_=ident[:, :], compare_op=ALU.not_equal, fill=1.0,
                                    base=0, pattern=[[-1, P]], channel_multiplier=1).then_inc(consts, 1)
            pool.wait_ge(consts, 2)

            def rstd(mv, r, k):
                nc.gpsimd.tensor_scalar(r[:, 0:1], mv[:, 1:2], EPS, None, ALU.add).then_inc(pool_step, 1)
                pool.wait_ge(pool_step, at(k + 1))
                return nc.gpsimd.tensor_tensor(r[:, 1:2], r[:, 0:1], half[:, :], ALU.pow)

            def x_rstd(j, k):
                pool.wait_ge(xag, at(j + 1))
                pool.sem_inc(passed)
                rstd(xmv, xrstd, k).then_inc(xr_done, 1)

            def y_rstd(j, k):
                pool.wait_ge(yag, at(j + 1))
                if not isinstance(j, int) or j >= 1:
                    pool.wait_ge(ynorm_done, at(j))
                pool.sem_inc(passed)
                rstd(ymv, yrstd, k).then_inc(pool_step, 1)
                pool.wait_ge(pool_step, at(k + 2))
                pool.sem_inc(passed)
                nc.gpsimd.tensor_scalar(ymean[:, :], ymv[:, 0:1], -1.0, None, ALU.mult).then_inc(pool_step, 1)
                pool.wait_ge(pool_step, at(k + 3))
                nc.gpsimd.tensor_tensor(ybias[:, :], ymean[:, :], yrstd[:, 1:2], ALU.mult).then_inc(pool_step, 1)
                pool.wait_ge(pool_step, at(k + 4))
                pool.sem_inc(passed)
                nc.gpsimd.tensor_copy(yrstd[:, 0:1], yrstd[:, 1:2]).then_inc(yr_done, 1)

            def first_guess(j, par):
                pool.wait_ge(a_done, at(j + 1))
                pool.sem_inc(passed)
                nc.gpsimd.tensor_scalar(unit[:, :], gains[:, :], asum[:, par:par + 1],
                                        1.0 / (2 * I * I * DENSITY), ALU.mult, ALU.mult)
                nc.gpsimd.tensor_scalar(thr[:, par:par + 1], asum[:, par:par + 1], GUESS / I, None,
                                        ALU.mult).then_inc(thr_done, 1)

            def newton(j, par, n, k):
                pool.wait_ge(counted, at(STEPS * j + j + n + 1))
                pool.wait_ge(thr_done, at(STEPS * j + j + n + 1))
                pool.sem_inc(passed)
                nc.gpsimd.tensor_scalar(err[:, :], sgn[:, par:par + 1], -1.0, float(2 * AIM - I),
                                        ALU.mult, ALU.add).then_inc(pool_step, 1)
                pool.wait_ge(pool_step, at(k + 1))
                pool.sem_inc(passed)
                nc.gpsimd.tensor_scalar(move[:, :], err[:, :], err[:, :], float((WINDOW - 1) ** 2) + 0.5,
                                        ALU.mult, ALU.is_gt).then_inc(pool_step, 1)
                pool.wait_ge(pool_step, at(k + 2))
                nc.gpsimd.tensor_tensor(delta[:, :], err[:, :], move[:, :], ALU.mult).then_inc(pool_step, 1)
                pool.wait_ge(pool_step, at(k + 3))
                pool.sem_inc(passed)
                nc.gpsimd.tensor_scalar(thr[:, par:par + 1], delta[:, :], unit[:, n:n + 1],
                                        thr[:, par:par + 1], ALU.mult, ALU.add).then_inc(thr_done, 1)

            XK, YK, NK = 1, 4, 3

            def step(j, par, b, prev, next_):
                static = isinstance(j, int)
                if static:
                    xs = 1 if j == 0 else j + 2 if j <= TILES else min(j + 1, T2)
                else:
                    xs = j + 2 if b == 0 else j + 1
                k = 1 + XK * xs + YK * (max(j - 2, 0) if static else j - 2) + NK * STEPS * (j if b == 0 else TILES)
                if static and j == 0 or next_ is not None and b == 1 and not (static and j == TILES):
                    x_rstd(j + 1, k)
                    k = k + XK
                if not static or j >= 2:
                    y_rstd(j - 2, k)
                    k = k + YK
                if b == 0:
                    first_guess(j, par)
                    x_at = STEPS if static and j in (0, TILES - 1) else STEPS - 1
                    for n in range(STEPS + 1):
                        if n == x_at:
                            x_rstd(j + 2, k)
                            k = k + XK
                        if n < STEPS:
                            newton(j, par, n, k)
                            k = k + NK

            x_rstd(0, 1)
            pipeline(pool, step)
            y_rstd(T2 - 1, 1 + XK * T2 + YK * (T2 - 1) + NK * STEPS * TILES)


CONSTS = 2

_INS = ["L0_attn_x", "L0_attn_w_gate", "L0_attn_w_up", "L0_attn_w_down",
        "L0_ffn_W_gate", "L0_ffn_W_up", "L0_ffn_W_down"]


def kernel(**inputs):
    import concourse.bacc as _bacc
    from concourse.bass_utils import run_bass_kernel_spmd as _run

    nc = _bacc.Bacc("TRN2", target_bir_lowering=False, num_devices=1)
    arrays, args = {}, []
    for name in _INS:
        a = np.ascontiguousarray(inputs[name])
        arrays[f"in_{name}"] = a
        args.append(nc.dram_tensor(f"in_{name}", a.shape, mybir.dt.from_np(a.dtype), kind="ExternalInput").ap())
    shape = inputs["L0_attn_x"].shape
    args.append(nc.dram_tensor("out_0", shape, F32, kind="ExternalOutput").ap())
    sandwich(nc, *args)
    r = _run(nc, [arrays], core_ids=[0])
    return r.results[0]["out_0"]
```
